# Optimizing a Trainium2 kernel written in Bass

```python
import numpy as np
import jax
import jax.numpy as jnp

def _softmax(x, axis=-1):
    return jax.nn.softmax(x, axis=axis)

def _gelu(x):
    return jax.nn.gelu(x, approximate=True)

def _silu(x):
    return jax.nn.silu(x)

def _sigmoid(x):
    return jax.nn.sigmoid(x)

def _layernorm(x, axis=-1, eps=1e-05):
    m = jnp.mean(x, axis=axis, keepdims=True)
    v = jnp.var(x, axis=axis, keepdims=True)
    return (x - m) / jnp.sqrt(v + eps)

def _scatter_add(tgt, idx, src, axis=0):
    return tgt.at[idx].add(src)

def _segment_sum(src, seg, n):
    return jax.ops.segment_sum(src, seg, n)
kernel_name = 'mk_dlrm_tower_d1_rec_r8_258692'

def setup_inputs(seed: int=0):
    np.random.seed(seed)
    _w = jnp.asarray

    def _rec_inputs():
        import jax
        import jax.numpy as jnp
        _tk = jax.random.key(seed)
        dense_ctx = jax.random.normal(jax.random.fold_in(_tk, 190), (512, 16), jnp.float32)
        ids = jnp.stack([jax.random.randint(jax.random.fold_in(_tk, 200 + f), (512,), 0, v, jnp.int32) for f, v in enumerate([1000, 1000, 1250, 1250, 12500, 1250, 12500, 125000, 125000, 1250, 1250, 12500, 12500, 1250, 125000, 12500, 1000, 1000, 1000, 12500, 1000, 1250, 1000, 1250, 12500, 12500, 1000, 1250, 1000, 1000, 1000, 1000])], axis=1)
        tbl_0 = 0.05 * jax.random.normal(jax.random.fold_in(_tk, 500 + 0), (1000, 64), jnp.float32)
        tbl_1 = 0.05 * jax.random.normal(jax.random.fold_in(_tk, 500 + 1), (1000, 64), jnp.float32)
        tbl_2 = 0.05 * jax.random.normal(jax.random.fold_in(_tk, 500 + 2), (1250, 64), jnp.float32)
        tbl_3 = 0.05 * jax.random.normal(jax.random.fold_in(_tk, 500 + 3), (1250, 64), jnp.float32)
        tbl_4 = 0.05 * jax.random.normal(jax.random.fold_in(_tk, 500 + 4), (12500, 64), jnp.float32)
        tbl_5 = 0.05 * jax.random.normal(jax.random.fold_in(_tk, 500 + 5), (1250, 64), jnp.float32)
        tbl_6 = 0.05 * jax.random.normal(jax.random.fold_in(_tk, 500 + 6), (12500, 64), jnp.float32)
        tbl_7 = 0.05 * jax.random.normal(jax.random.fold_in(_tk, 500 + 7), (125000, 64), jnp.float32)
        tbl_8 = 0.05 * jax.random.normal(jax.random.fold_in(_tk, 500 + 8), (125000, 64), jnp.float32)
        tbl_9 = 0.05 * jax.random.normal(jax.random.fold_in(_tk, 500 + 9), (1250, 64), jnp.float32)
        tbl_10 = 0.05 * jax.random.normal(jax.random.fold_in(_tk, 500 + 10), (1250, 64), jnp.float32)
        tbl_11 = 0.05 * jax.random.normal(jax.random.fold_in(_tk, 500 + 11), (12500, 64), jnp.float32)
        tbl_12 = 0.05 * jax.random.normal(jax.random.fold_in(_tk, 500 + 12), (12500, 64), jnp.float32)
        tbl_13 = 0.05 * jax.random.normal(jax.random.fold_in(_tk, 500 + 13), (1250, 64), jnp.float32)
        tbl_14 = 0.05 * jax.random.normal(jax.random.fold_in(_tk, 500 + 14), (125000, 64), jnp.float32)
        tbl_15 = 0.05 * jax.random.normal(jax.random.fold_in(_tk, 500 + 15), (12500, 64), jnp.float32)
        tbl_16 = 0.05 * jax.random.normal(jax.random.fold_in(_tk, 500 + 16), (1000, 64), jnp.float32)
        tbl_17 = 0.05 * jax.random.normal(jax.random.fold_in(_tk, 500 + 17), (1000, 64), jnp.float32)
        tbl_18 = 0.05 * jax.random.normal(jax.random.fold_in(_tk, 500 + 18), (1000, 64), jnp.float32)
        tbl_19 = 0.05 * jax.random.normal(jax.random.fold_in(_tk, 500 + 19), (12500, 64), jnp.float32)
        tbl_20 = 0.05 * jax.random.normal(jax.random.fold_in(_tk, 500 + 20), (1000, 64), jnp.float32)
        tbl_21 = 0.05 * jax.random.normal(jax.random.fold_in(_tk, 500 + 21), (1250, 64), jnp.float32)
        tbl_22 = 0.05 * jax.random.normal(jax.random.fold_in(_tk, 500 + 22), (1000, 64), jnp.float32)
        tbl_23 = 0.05 * jax.random.normal(jax.random.fold_in(_tk, 500 + 23), (1250, 64), jnp.float32)
        tbl_24 = 0.05 * jax.random.normal(jax.random.fold_in(_tk, 500 + 24), (12500, 64), jnp.float32)
        tbl_25 = 0.05 * jax.random.normal(jax.random.fold_in(_tk, 500 + 25), (12500, 64), jnp.float32)
        tbl_26 = 0.05 * jax.random.normal(jax.random.fold_in(_tk, 500 + 26), (1000, 64), jnp.float32)
        tbl_27 = 0.05 * jax.random.normal(jax.random.fold_in(_tk, 500 + 27), (1250, 64), jnp.float32)
        tbl_28 = 0.05 * jax.random.normal(jax.random.fold_in(_tk, 500 + 28), (1000, 64), jnp.float32)
        tbl_29 = 0.05 * jax.random.normal(jax.random.fold_in(_tk, 500 + 29), (1000, 64), jnp.float32)
        tbl_30 = 0.05 * jax.random.normal(jax.random.fold_in(_tk, 500 + 30), (1000, 64), jnp.float32)
        tbl_31 = 0.05 * jax.random.normal(jax.random.fold_in(_tk, 500 + 31), (1000, 64), jnp.float32)
        _rk = jax.random.fold_in(_tk, 7)
        W_top1 = 0.0441942 * jax.random.normal(jax.random.fold_in(_tk, 801), (512, 512), jnp.float32)
        W_top2 = 0.0441942 * jax.random.normal(jax.random.fold_in(_tk, 802), (512, 256), jnp.float32)
        W_top3 = 0.0625 * jax.random.normal(jax.random.fold_in(_tk, 803), (256, 1), jnp.float32)
        b_top1 = jnp.zeros((512,), jnp.float32)
        b_top2 = jnp.zeros((256,), jnp.float32)
        return (dense_ctx, ids, tbl_0, tbl_1, tbl_2, tbl_3, tbl_4, tbl_5, tbl_6, tbl_7, tbl_8, tbl_9, tbl_10, tbl_11, tbl_12, tbl_13, tbl_14, tbl_15, tbl_16, tbl_17, tbl_18, tbl_19, tbl_20, tbl_21, tbl_22, tbl_23, tbl_24, tbl_25, tbl_26, tbl_27, tbl_28, tbl_29, tbl_30, tbl_31, W_top1, b_top1, W_top2, b_top2, W_top3)
    dense_ctx, ids, tbl_0, tbl_1, tbl_2, tbl_3, tbl_4, tbl_5, tbl_6, tbl_7, tbl_8, tbl_9, tbl_10, tbl_11, tbl_12, tbl_13, tbl_14, tbl_15, tbl_16, tbl_17, tbl_18, tbl_19, tbl_20, tbl_21, tbl_22, tbl_23, tbl_24, tbl_25, tbl_26, tbl_27, tbl_28, tbl_29, tbl_30, tbl_31, W_top1, b_top1, W_top2, b_top2, W_top3 = _rec_inputs()

    def _L0_rec_setup():
        import jax, jax.numpy as jnp
        import numpy as np
        B = 256
        NUM_FIELDS = 32
        EMBED = 64
        P = NUM_FIELDS * (NUM_FIELDS - 1) // 2
        _ROW, _COL = np.triu_indices(NUM_FIELDS, k=1)
        ROW_IDX = jnp.asarray(_ROW, dtype=jnp.int32)
        COL_IDX = jnp.asarray(_COL, dtype=jnp.int32)
        key = jax.random.key(seed)
        k1, k2 = jax.random.split(key)
        emb_inputs = jax.random.normal(k1, (B, NUM_FIELDS, EMBED), dtype=jnp.float32)
        fan_in = P * EMBED
        fan_out = EMBED
        std = float(np.sqrt(2.0 / (fan_in + fan_out)))
        kernel = jax.random.normal(k2, (EMBED, P, EMBED), dtype=jnp.float32) * std
        return {'emb_inputs': emb_inputs, 'kernel': kernel}
    _L0_rec_all = _L0_rec_setup()
    _L0_rec_in = {k: v for k, v in _L0_rec_all.items() if k in ('kernel',)}
    del _L0_rec_all
    return {'dense_ctx': dense_ctx, 'ids': ids, 'tbl_0': tbl_0, 'tbl_1': tbl_1, 'tbl_2': tbl_2, 'tbl_3': tbl_3, 'tbl_4': tbl_4, 'tbl_5': tbl_5, 'tbl_6': tbl_6, 'tbl_7': tbl_7, 'tbl_8': tbl_8, 'tbl_9': tbl_9, 'tbl_10': tbl_10, 'tbl_11': tbl_11, 'tbl_12': tbl_12, 'tbl_13': tbl_13, 'tbl_14': tbl_14, 'tbl_15': tbl_15, 'tbl_16': tbl_16, 'tbl_17': tbl_17, 'tbl_18': tbl_18, 'tbl_19': tbl_19, 'tbl_20': tbl_20, 'tbl_21': tbl_21, 'tbl_22': tbl_22, 'tbl_23': tbl_23, 'tbl_24': tbl_24, 'tbl_25': tbl_25, 'tbl_26': tbl_26, 'tbl_27': tbl_27, 'tbl_28': tbl_28, 'tbl_29': tbl_29, 'tbl_30': tbl_30, 'tbl_31': tbl_31, 'W_top1': W_top1, 'b_top1': b_top1, 'W_top2': W_top2, 'b_top2': b_top2, 'W_top3': W_top3, 'L0_rec_kernel': _L0_rec_in['kernel']}

def reference(dense_ctx, ids, tbl_0, tbl_1, tbl_2, tbl_3, tbl_4, tbl_5, tbl_6, tbl_7, tbl_8, tbl_9, tbl_10, tbl_11, tbl_12, tbl_13, tbl_14, tbl_15, tbl_16, tbl_17, tbl_18, tbl_19, tbl_20, tbl_21, tbl_22, tbl_23, tbl_24, tbl_25, tbl_26, tbl_27, tbl_28, tbl_29, tbl_30, tbl_31, W_top1, b_top1, W_top2, b_top2, W_top3, L0_rec_kernel):
    import jax
    import jax.numpy as jnp

    def _L0_rec_ref(emb_inputs, kernel):
        import jax, jax.numpy as jnp
        import numpy as np
        B = 256
        NUM_FIELDS = 32
        EMBED = 64
        P = NUM_FIELDS * (NUM_FIELDS - 1) // 2
        _ROW, _COL = np.triu_indices(NUM_FIELDS, k=1)
        ROW_IDX = jnp.asarray(_ROW, dtype=jnp.int32)
        COL_IDX = jnp.asarray(_COL, dtype=jnp.int32)
        p = emb_inputs[:, ROW_IDX]
        q = emb_inputs[:, COL_IDX]
        return jnp.einsum('bne,hne,bnh->bn', p, kernel, q)
    e = jnp.stack([tbl_0[ids[:, 0]], tbl_1[ids[:, 1]], tbl_2[ids[:, 2]], tbl_3[ids[:, 3]], tbl_4[ids[:, 4]], tbl_5[ids[:, 5]], tbl_6[ids[:, 6]], tbl_7[ids[:, 7]], tbl_8[ids[:, 8]], tbl_9[ids[:, 9]], tbl_10[ids[:, 10]], tbl_11[ids[:, 11]], tbl_12[ids[:, 12]], tbl_13[ids[:, 13]], tbl_14[ids[:, 14]], tbl_15[ids[:, 15]], tbl_16[ids[:, 16]], tbl_17[ids[:, 17]], tbl_18[ids[:, 18]], tbl_19[ids[:, 19]], tbl_20[ids[:, 20]], tbl_21[ids[:, 21]], tbl_22[ids[:, 22]], tbl_23[ids[:, 23]], tbl_24[ids[:, 24]], tbl_25[ids[:, 25]], tbl_26[ids[:, 26]], tbl_27[ids[:, 27]], tbl_28[ids[:, 28]], tbl_29[ids[:, 29]], tbl_30[ids[:, 30]], tbl_31[ids[:, 31]]], axis=1)
    z = _L0_rec_ref(e, L0_rec_kernel)
    z = z.reshape(z.shape[0], -1)
    h = jnp.concatenate([z, dense_ctx], axis=1)
    h = jnp.maximum(h @ W_top1 + b_top1, 0.0)
    h = jnp.maximum(h @ W_top2 + b_top2, 0.0)
    y = h @ W_top3
    return y

_drawn_inputs = setup_inputs


def setup_inputs(seed=0):
    import zlib

    import numpy as np

    out = dict(_drawn_inputs(seed))
    spreads = {'b_top1': (0.0, 0.1), 'b_top2': (0.0, 0.1)}
    factors = {'tbl_0': 8.0,
     'tbl_1': 8.0,
     'tbl_2': 8.0,
     'tbl_3': 8.0,
     'tbl_4': 8.0,
     'tbl_5': 8.0,
     'tbl_6': 8.0,
     'tbl_7': 8.0,
     'tbl_8': 8.0,
     'tbl_9': 8.0,
     'tbl_10': 8.0,
     'tbl_11': 8.0,
     'tbl_12': 8.0,
     'tbl_13': 8.0,
     'tbl_14': 8.0,
     'tbl_15': 8.0,
     'tbl_16': 8.0,
     'tbl_17': 8.0,
     'tbl_18': 8.0,
     'tbl_19': 8.0,
     'tbl_20': 8.0,
     'tbl_21': 8.0,
     'tbl_22': 8.0,
     'tbl_23': 8.0,
     'tbl_24': 8.0,
     'tbl_25': 8.0,
     'tbl_26': 8.0,
     'tbl_27': 8.0,
     'tbl_28': 8.0,
     'tbl_29': 8.0,
     'tbl_30': 8.0,
     'tbl_31': 8.0,
     'L0_rec_kernel': 8.0}
    for name, (base, spread) in spreads.items():
        noise = np.random.default_rng([zlib.crc32(name.encode()), seed]).standard_normal(out[name].shape)
        drawn = base * np.exp(spread * noise) if base else spread * noise
        out[name] = jnp.asarray(drawn.astype(out[name].dtype))
    for name, factor in factors.items():
        out[name] = (out[name] * factor).astype(out[name].dtype)
    return out
```

```python
from contextlib import ExitStack

import concourse.bass as bass
from concourse import mybir

FP32 = mybir.dt.float32
FP32R = mybir.dt.float32r
INT32 = mybir.dt.int32
ALU = mybir.AluOpType
ACT = mybir.ActivationFunctionType
AX_X = mybir.AxisListType.X

P = 128
FIELDS = 32
EMB = 64
NPAIR = FIELDS * (FIELDS - 1) // 2
GROUP = 4
NGROUP = FIELDS // GROUP
KCOLS = NPAIR * EMB
KCHUNK = 16
CW = KCOLS // KCHUNK
HW = CW // 2
BANK = 512
PIECE = 2 * BANK
SLOTS = 3
PRODS = 6
RAWS = 3
PART = 8


def pair_column(i, j):
    return j * (j - 1) // 2 + i


def plan_pieces():
    pieces = [[(1, 0, 1), (2, 0, 2), (3, 0, 3)], [(4, 0, 4), (5, 0, 5)], [(6, 0, 6), (7, 0, 7)]]
    for j in range(8, FIELDS):
        pieces.append([(j, 0, min(j, 16))])
        if j > 16:
            pieces.append([(j, 16, j)])
    return pieces


def plan_reductions(pieces, last_tile):
    load = {"V": 0.0, "A": 0.0, "T": 0.0}
    kinds = []
    for k, piece in enumerate(pieces):
        n = sum(i1 - i0 for _, i0, i1 in piece)
        load["V"] += 0.0667 * n + 0.068 * len(piece) + 0.09
        load["T"] += 0.056 * n + 0.12
        load["A"] += 0.12
        cost = {"V": 0.0667 * n + 0.068, "A": 0.24 * n, "T": 0.11 * n}
        can = ["V", "A"] + (["T"] if n >= 12 else [])
        if last_tile and k >= len(pieces) - 3:
            can = ["V"]
        best = min(can, key=lambda e: load[e] + cost[e])
        load[best] += cost[best]
        if best == "T":
            load["V"] += 0.2
        kinds.append(best)
    return kinds


def dlrm_tower(nc, dense, ids, tables, k_raw, w1, b1, w2, b2, w3, ident_in, y_out):
    TILES = ids.shape[1]
    D1 = w1.shape[2]
    D2 = w2.shape[2]
    A1, A2 = w1.shape[1], w2.shape[1]
    M1, M2 = D1 // P, D2 // P
    NDENSE = dense.shape[2]

    pieces = plan_pieces()
    NP = len(pieces)
    kinds = [plan_reductions(pieces, t == TILES - 1) for t in range(TILES)]
    width = [sum(i1 - i0 for _, i0, i1 in piece) for piece in pieces]
    col0 = [pair_column(piece[0][1], piece[0][0]) for piece in pieces]
    group_of = [piece[0][0] // GROUP for piece in pieces]
    first_piece = [group_of.index(g) for g in range(NGROUP)]
    chunk_of = [-(-(col0[k] + width[k]) * EMB // CW) - 1 for k in range(NP)]

    def count(kind, t, k):
        n = sum(kinds[s].count(kind) for s in range(t))
        return n + kinds[t][:k + 1].count(kind)

    with ExitStack() as ctx:
        def sb(name, shape, dt=FP32):
            return ctx.enter_context(nc.sbuf_tensor(name, shape, dt))

        def psum(name, shape):
            return ctx.enter_context(nc.psum_tensor(name, shape, FP32))

        def sem(name):
            return ctx.enter_context(nc.semaphore(name))

        ksplit = sb("ksplit", [P, KCOLS], FP32R)
        early = sb("early", [P, max(RAWS * HW, A1 * D1 + A2 * D2)])
        kraw = early[:, 0:RAWS * HW].rearrange("p (s n) -> p s n", s=RAWS)
        w1_sb = early[:, 0:A1 * D1].rearrange("p (a m) -> p a m", a=A1)
        w2_sb = early[:, A1 * D1:A1 * D1 + A2 * D2].rearrange("p (a m) -> p a m", a=A2)
        ids_sb = sb("ids_sb", [P, TILES, FIELDS], INT32)
        emb = sb("emb", [P, 2, FIELDS, EMB])
        twice = sb("twice", [P, 2, GROUP, 2, EMB])
        qhi = sb("qhi", [P, 2, GROUP * P], FP32R)
        qlo = sb("qlo", [P, 2, GROUP * P], FP32R)
        prod = sb("prod", [P, PRODS, PIECE])
        z = sb("z", [P, TILES, D1])
        ident = sb("ident", [P, P])
        w3_sb = sb("w3_sb", [P, M2])
        b1_sb = sb("b1_sb", [P, M1])
        b2_sb = sb("b2_sb", [P, M2])
        act_t = sb("act_t", [P, D1])
        h1_t = sb("h1_t", [P, D1])
        h2_t = sb("h2_t", [P, D2])
        y_sb = sb("y_sb", [1, TILES * P])

        ps_t = psum("ps_t", [P, SLOTS, PIECE])
        ps_q = psum("ps_q", [P, GROUP * P])
        ps_m = psum("ps_m", [P, BANK])

        ids_in = sem("ids_in")
        ident_sem = sem("ident_sem")
        weights_in = sem("weights_in")
        dense_in = sem("dense_in")
        raw_in = [sem(f"raw_in{s}") for s in range(RAWS)]
        emb_in = [[sem(f"emb_in{b}_{g}") for g in range(NGROUP)] for b in range(2)]
        khi_done = sem("khi_done")
        klo_done = sem("klo_done")
        twice_done = sem("twice_done")
        turned = sem("turned")
        qhi_done = sem("qhi_done")
        qlo_done = sem("qlo_done")
        pairs_done = sem("pairs_done")
        mult_done = sem("mult_done")
        vsum_done = sem("vsum_done")
        asum_done = sem("asum_done")
        tsum_done = sem("tsum_done")
        tfinal_done = sem("tfinal_done")
        tower_mm = sem("tower_mm")
        tower_act = sem("tower_act")
        y_stored = sem("y_stored")

        TOWER = 4
        TOWER_AT = [6, 9, 12, 15]
        T_LAG = 3
        F_LAG = 4

        def side_steps(t, k):
            steps = []
            if t < TILES and k - T_LAG >= 0 and kinds[t][k - T_LAG] == "T":
                steps.append(("T", t, k - T_LAG))
            if t > 0 and k < T_LAG and kinds[t - 1][NP + k - T_LAG] == "T":
                steps.append(("T", t - 1, NP + k - T_LAG))
            if t > 0 and k in TOWER_AT:
                steps.append(("M", t - 1, TOWER_AT.index(k)))
            return steps

        users = [u for t in range(TILES + 1) for k in range(NP if t < TILES else TOWER_AT[-1] + 1)
                 for u in side_steps(t, k)]
        assert len(set(users)) == len(users)

        def wait_ps_m_free(pe, user):
            n = users.index(user)
            if n == 0:
                return
            kind, t, k = users[n - 1]
            if kind == "T":
                pe.wait_ge(tfinal_done, count("T", t, k))
            else:
                pe.wait_ge(tower_act, t * TOWER + k + 1)

        K_AHEAD = 4

        def chunks_at(k):
            if k < 0:
                return range(0, K_AHEAD)
            return range(K_AHEAD + k, K_AHEAD + k + 1) if K_AHEAD + k < KCHUNK else range(0)

        block = ctx.enter_context(nc.Block())

        @block.sync
        def _(sp):
            sp.dma_start(ids_sb[:], ids).then_inc(ids_in, 16)
            for c in range(KCHUNK):
                if c >= RAWS:
                    sp.wait_ge(klo_done, c - RAWS + 1)
                sp.dma_start(kraw[:, c % RAWS, :], k_raw[c]).then_inc(raw_in[c % RAWS], 16)
                if c == 0:
                    sp.dma_start(ident[:], ident_in).then_inc(ident_sem, 16)
            sp.dma_start(z[:, :, NPAIR:NPAIR + NDENSE], dense).then_inc(dense_in, 16)
            sp.wait_ge(klo_done, KCHUNK)
            sp.dma_start(w1_sb, w1).then_inc(weights_in, 16)
            sp.dma_start(w2_sb, w2).then_inc(weights_in, 16)
            sp.dma_start(w3_sb[:], w3).then_inc(weights_in, 16)
            sp.dma_start(b1_sb[:], b1).then_inc(weights_in, 16)
            sp.dma_start(b2_sb[:], b2).then_inc(weights_in, 16)
            sp.wait_ge(tower_act, TILES * TOWER)
            sp.dma_start(y_out, y_sb[:]).then_inc(y_stored, 16)
            sp.wait_ge(y_stored, 16)

        @block.gpsimd
        def _(pool):
            pool.wait_ge(ids_in, 16)
            for t in range(TILES):
                if t >= 2:
                    pool.wait_ge(mult_done, (t - 1) * NP)
                for f in range(FIELDS):
                    pool.indirect_dma_start(
                        emb[:, t % 2, f, :], None, tables[f],
                        bass.IndirectOffsetOnAxis(ap=ids_sb[:, t, f:f + 1], axis=0),
                    ).then_inc(emb_in[t % 2][f // GROUP], 16)

        def wait_emb(eng, t, g):
            eng.wait_ge(emb_in[t % 2][g], 16 * GROUP * (t // 2 + 1))

        @block.scalar
        def _(act):
            def split_chunk(c):
                act.wait_ge(raw_in[c % RAWS], 16 * (c // RAWS + 1))
                for half in range(2):
                    o = c * CW + half * HW
                    rows = slice(half * 64, half * 64 + 64)
                    last = act.activation(ksplit[rows, o:o + HW], kraw[rows, c % RAWS, :], ACT.Copy)
                last.then_inc(khi_done, 1)

            def double_rows(n):
                t, g = divmod(n, NGROUP)
                wait_emb(act, t, g)
                if n >= 2:
                    act.wait_ge(turned, n - 1)
                src = emb[:, t % 2, GROUP * g:GROUP * (g + 1), :]
                act.activation(twice[:, n % 2], src.unsqueeze(2).broadcast_to([P, GROUP, 2, EMB]),
                               ACT.Copy).then_inc(twice_done, 1)

            def high_q(n):
                t, g = divmod(n, NGROUP)
                act.wait_ge(turned, n + 1)
                if n >= 2:
                    s, h = divmod(n - 2, NGROUP)
                    act.wait_ge(pairs_done, s * NP + (first_piece[h + 1] if h + 1 < NGROUP else NP))
                act.activation(qhi[:, n % 2], ps_q[:], ACT.Copy).then_inc(qhi_done, 1)

            def tower(t, step):
                act.wait_ge(tower_mm, t * TOWER + step + 1)
                if step == 0:
                    last = act.activation(act_t[:], ps_m[:], ACT.Copy)
                elif step == 1:
                    act.wait_ge(weights_in, 80)
                    for m in range(M1):
                        last = act.activation(h1_t[:, m * P:(m + 1) * P], ps_m[:, m * P:(m + 1) * P],
                                              ACT.Relu, bias=b1_sb[:, m:m + 1])
                elif step == 2:
                    for m in range(M2):
                        last = act.activation(h2_t[:, m * P:(m + 1) * P], ps_m[:, m * P:(m + 1) * P],
                                              ACT.Relu, bias=b2_sb[:, m:m + 1])
                else:
                    last = act.activation(y_sb[:, t * P:(t + 1) * P], ps_m[0:1, 0:P], ACT.Copy)
                last.then_inc(tower_act, 1)

            def sum_piece(t, k):
                act.wait_ge(mult_done, t * NP + k + 1)
                for c in range(width[k]):
                    src = prod[:, (t * NP + k) % PRODS, c * EMB:(c + 1) * EMB]
                    last = act.activation(src, src, ACT.Copy, accum_out=z[:, t, col0[k] + c:col0[k] + c + 1])
                last.then_inc(asum_done, 1)

            for c in chunks_at(-1):
                split_chunk(c)
            double_rows(0)
            high_q(0)
            for t in range(TILES):
                for k in range(NP):
                    g = group_of[k]
                    n = t * NGROUP + g + 1
                    if t > 0 and k in TOWER_AT:
                        tower(t - 1, TOWER_AT.index(k))
                    if k == first_piece[g] and n < TILES * NGROUP:
                        double_rows(n)
                    if k == first_piece[g] and n < TILES * NGROUP:
                        high_q(n)
                    if t == 0:
                        for c in chunks_at(k):
                            split_chunk(c)
                    if kinds[t][k] == "A":
                        sum_piece(t, k)
            for step in range(TOWER):
                tower(TILES - 1, step)

        @block.vector
        def _(dve):
            def split_chunk(c):
                dve.wait_ge(khi_done, c + 1)
                for half in range(2):
                    o = c * CW + half * HW
                    rows = slice(half * 64, half * 64 + 64)
                    other = slice(64 - half * 64, 128 - half * 64)
                    last = dve.tensor_tensor(ksplit[other, o:o + HW], kraw[rows, c % RAWS, :],
                                             ksplit[rows, o:o + HW], ALU.subtract)
                last.then_inc(klo_done, 1)

            def low_q(n):
                dve.wait_ge(qhi_done, n + 1)
                dve.tensor_tensor(qlo[:, n % 2], ps_q[:], qhi[:, n % 2], ALU.subtract).then_inc(qlo_done, 1)

            def multiply(t, k):
                n = t * NP + k
                if n >= PRODS:
                    s, h = divmod(n - PRODS, NP)
                    done = {"V": vsum_done, "A": asum_done, "T": tsum_done}[kinds[s][h]]
                    dve.wait_ge(done, count(kinds[s][h], s, h))
                dve.wait_ge(pairs_done, n + 1)
                o = 0
                for j, i0, i1 in pieces[k]:
                    w = (i1 - i0) * EMB
                    last = dve.tensor_tensor(
                        prod[:, n % PRODS, o:o + w], ps_t[:, n % SLOTS, o:o + w],
                        emb[:, t % 2, i0:i1, :].rearrange("p i e -> p (i e)"), ALU.mult)
                    o += w
                last.then_inc(mult_done, 1)

            def sum_piece(t, k):
                dve.wait_ge(mult_done, t * NP + k + 1)
                src = prod[:, (t * NP + k) % PRODS, 0:width[k] * EMB].rearrange("p (n e) -> p n e", e=EMB)
                dve.tensor_reduce(z[:, t, col0[k]:col0[k] + width[k]], src, AX_X, ALU.add).then_inc(vsum_done, 1)

            def finish_sum(t, k):
                dve.wait_ge(tsum_done, count("T", t, k))
                src = ps_m[:, 0:width[k] * PART].rearrange("p (n r) -> p n r", r=PART)
                dve.tensor_reduce(z[:, t, col0[k]:col0[k] + width[k]], src, AX_X, ALU.add).then_inc(tfinal_done, 1)

            for c in chunks_at(-1):
                split_chunk(c)
            low_q(0)
            for t in range(TILES):
                for k in range(NP):
                    multiply(t, k)
                    if t == 0:
                        for c in chunks_at(k):
                            split_chunk(c)
                    for lag, kind, do in ((1, "V", sum_piece), (F_LAG, "T", finish_sum)):
                        s, h = divmod(t * NP + k - lag, NP)
                        if s >= 0 and kinds[s][h] == kind:
                            do(s, h)
                    g = group_of[k]
                    n = t * NGROUP + g + 1
                    if k == first_piece[g] and n < TILES * NGROUP:
                        low_q(n)
            t = TILES - 1
            for lag, kind, do in ((F_LAG, "T", finish_sum), (1, "V", sum_piece)):
                for h in range(NP - lag, NP):
                    if kinds[t][h] == kind:
                        do(t, h)

        @block.tensor
        def _(pe):
            def turn(n):
                pe.wait_ge(twice_done, n + 1)
                if n >= 1:
                    pe.wait_ge(qlo_done, n)
                for f in range(GROUP):
                    last = pe.transpose(ps_q[:, f * P:(f + 1) * P],
                                        twice[:, n % 2, f].rearrange("p a e -> p (a e)"), ident[:])
                last.then_inc(turned, 1)

            def bilinear(t, k):
                n = t * NP + k
                if k == first_piece[group_of[k]]:
                    pe.wait_ge(qlo_done, t * NGROUP + group_of[k] + 1)
                if t == 0:
                    pe.wait_ge(klo_done, chunk_of[k] + 1)
                if n >= SLOTS:
                    pe.wait_ge(mult_done, n - SLOTS + 1)
                q = (t * NGROUP + group_of[k]) % 2
                o = 0
                for j, i0, i1 in pieces[k]:
                    f = j % GROUP
                    i = i0
                    while i < i1:
                        w = min((i1 - i) * EMB, BANK - o % BANK)
                        src = pair_column(i, j) * EMB
                        dst = ps_t[:, n % SLOTS, o:o + w]
                        pe.matmul(dst, qhi[:, q, f * P:(f + 1) * P], ksplit[:, src:src + w],
                                  start=True, stop=False)
                        last = pe.matmul(dst, qlo[:, q, f * P:(f + 1) * P], ksplit[:, src:src + w],
                                         start=False, stop=True)
                        o += w
                        i += w // EMB
                last.then_inc(pairs_done, 1)

            def sum_piece(t, k):
                wait_ps_m_free(pe, ("T", t, k))
                pe.wait_ge(mult_done, t * NP + k + 1)
                w = width[k]
                src = prod[:, (t * NP + k) % PRODS, 0:w * EMB].rearrange("p (n s r) -> p s n r", n=w, r=PART)
                dst = ps_m[:, 0:w * PART].rearrange("p (n r) -> p n r", r=PART)
                for s in range(EMB // PART):
                    last = pe.matmul(dst, ident[:], src[:, s], start=(s == 0), stop=(s == EMB // PART - 1))
                last.then_inc(tsum_done, 1)

            def tower(t, step):
                wait_ps_m_free(pe, ("M", t, step))
                if step == 0:
                    pe.wait_ge(vsum_done, count("V", t, NP - 1))
                    pe.wait_ge(asum_done, count("A", t, NP - 1))
                    pe.wait_ge(tfinal_done, count("T", t, NP - 1))
                    pe.wait_ge(dense_in, 16)
                    for a in range(A1):
                        last = pe.transpose(ps_m[:, a * P:(a + 1) * P], z[:, t, a * P:(a + 1) * P], ident[:])
                elif step == 1:
                    pe.wait_ge(weights_in, 80)
                    pe.wait_ge(tower_act, t * TOWER + step)
                    for m in range(M1):
                        for a in range(A1):
                            last = pe.matmul(ps_m[:, m * P:(m + 1) * P], w1_sb[:, a, m * P:(m + 1) * P],
                                             act_t[:, a * P:(a + 1) * P], start=(a == 0), stop=(a == A1 - 1))
                elif step == 2:
                    pe.wait_ge(tower_act, t * TOWER + step)
                    for m in range(M2):
                        for a in range(A2):
                            last = pe.matmul(ps_m[:, m * P:(m + 1) * P], w2_sb[:, a, m * P:(m + 1) * P],
                                             h1_t[:, a * P:(a + 1) * P], start=(a == 0), stop=(a == A2 - 1))
                else:
                    pe.wait_ge(tower_act, t * TOWER + step)
                    for a in range(M2):
                        last = pe.matmul(ps_m[0:1, 0:P], w3_sb[:, a:a + 1], h2_t[:, a * P:(a + 1) * P],
                                         start=(a == 0), stop=(a == M2 - 1))
                last.then_inc(tower_mm, 1)

            def side(t, k):
                for kind, s, what in side_steps(t, k):
                    (sum_piece if kind == "T" else tower)(s, what)

            pe.wait_ge(ident_sem, 16)
            turn(0)
            for t in range(TILES):
                for k in range(NP):
                    bilinear(t, k)
                    g = group_of[k]
                    n = t * NGROUP + g + 1
                    if k == first_piece[g] and n < TILES * NGROUP:
                        turn(n)
                    side(t, k)
            for k in range(TOWER_AT[-1] + 1):
                side(TILES, k)


def kernel(dense_ctx, ids, W_top1, b_top1, W_top2, b_top2, W_top3, L0_rec_kernel, **tbls):
    import numpy as np
    import concourse.bacc as bacc
    from concourse.bass_utils import run_bass_kernel_spmd

    batch = ids.shape[0]
    tiles = batch // P
    row, col = np.triu_indices(FIELDS, k=1)
    order = np.lexsort((row, col))
    k = np.asarray(L0_rec_kernel)[:, order, :].reshape(EMB, KCHUNK, 2, HW)
    w1 = np.asarray(W_top1)
    w1 = np.concatenate([w1[:NPAIR][order], w1[NPAIR:]], axis=0)
    w2 = np.asarray(W_top2)

    def by_partition(a):
        return np.ascontiguousarray(a.reshape(-1, P, a.shape[1]).transpose(1, 0, 2))

    ins = {
        "dense": by_partition(np.asarray(dense_ctx)),
        "ids": by_partition(np.asarray(ids)),
        **{f"tbl_{f}": np.ascontiguousarray(tbls[f"tbl_{f}"]) for f in range(FIELDS)},
        "k_raw": np.ascontiguousarray(k.transpose(1, 2, 0, 3).reshape(KCHUNK, P, HW)),
        "w1": by_partition(w1),
        "b1": np.ascontiguousarray(np.asarray(b_top1).reshape(-1, P).T),
        "w2": by_partition(w2),
        "b2": np.ascontiguousarray(np.asarray(b_top2).reshape(-1, P).T),
        "w3": np.ascontiguousarray(np.asarray(W_top3).reshape(-1, P).T),
        "identity": np.eye(P, dtype=np.float32),
    }
    nc = bacc.Bacc("TRN2", target_bir_lowering=False, num_devices=1)
    ap = {n: nc.dram_tensor(n, a.shape, mybir.dt.from_np(a.dtype), kind="ExternalInput").ap() for n, a in ins.items()}
    y = nc.dram_tensor("y", (1, batch), FP32, kind="ExternalOutput").ap()
    dlrm_tower(nc, ap["dense"], ap["ids"], [ap[f"tbl_{f}"] for f in range(FIELDS)], ap["k_raw"], ap["w1"], ap["b1"],
               ap["w2"], ap["b2"], ap["w3"], ap["identity"], y)
    out = run_bass_kernel_spmd(nc, [ins], core_ids=[0])
    return out.results[0]["y"].reshape(batch, 1)
```

```python
from contextlib import ExitStack

import concourse.bass as bass
from concourse import mybir

FP32 = mybir.dt.float32
FP32R = mybir.dt.float32r
INT32 = mybir.dt.int32
ALU = mybir.AluOpType
ACT = mybir.ActivationFunctionType
AX_X = mybir.AxisListType.X

P = 128
FIELDS = 32
EMB = 64
NPAIR = FIELDS * (FIELDS - 1) // 2
GROUP = 4
NGROUP = FIELDS // GROUP
KCOLS = NPAIR * EMB
KCHUNK = 16
CW = KCOLS // KCHUNK
HW = CW // 2
BANK = 512
PIECE = 2 * BANK
SLOTS = 3
PRODS = 6
RAWS = 3
QS = 4
PART = 8


def pair_column(i, j):
    return j * (j - 1) // 2 + i


def plan_pieces():
    pieces = [[(1, 0, 1), (2, 0, 2), (3, 0, 3)], [(4, 0, 4), (5, 0, 5)], [(6, 0, 6), (7, 0, 7)]]
    for j in range(8, FIELDS):
        pieces.append([(j, 0, min(j, 16))])
        if j > 16:
            pieces.append([(j, 16, j)])
    return pieces


def plan_reductions(pieces, tile, tiles, not_t):
    load = {"V": 0.0, "A": 0.0, "T": 0.0, "G": 0.0}
    kinds = []
    for k, piece in enumerate(pieces):
        n = sum(i1 - i0 for _, i0, i1 in piece)
        load["V"] += 0.0667 * n + 0.068 * len(piece) + (0.11 if tile else 0.9)
        load["T"] += 0.060 * n + 0.22
        load["A"] += 0.2 if tile else 0.9
        load["G"] += 0.8
        cost = {"V": 0.0667 * n + 0.068, "A": 0.24 * n, "T": 0.11 * n, "G": 0.122 * n + 0.3}
        can = ["V", "A"] + (["T", "G"] if n >= 12 else [])
        if tile and k in not_t:
            can.remove("T") if "T" in can else None
        if tile == tiles - 1 and k >= len(pieces) - 3:
            can = ["V"]
        best = min(can, key=lambda e: load[e] + cost[e])
        load[best] += cost[best]
        if best in "TG":
            load["V"] += 0.2
        kinds.append(best)
    return kinds


def dlrm_tower(nc, dense, ids, tables, k_raw, w1, b1, w2, b2, w3, ident_in, y_out):
    TILES = ids.shape[1]
    D1 = w1.shape[2]
    D2 = w2.shape[2]
    A1, A2 = w1.shape[1], w2.shape[1]
    M1, M2 = D1 // P, D2 // P
    NDENSE = dense.shape[2]

    TOWER = 4
    TOWER_AT = [6, 9, 12, 15]
    T_LAG = 3
    G_LAG = 4
    F_LAG = 4
    NOT_T = [at - T_LAG for at in TOWER_AT]

    pieces = plan_pieces()
    NP = len(pieces)
    kinds = [plan_reductions(pieces, t, TILES, NOT_T) for t in range(TILES)]
    width = [sum(i1 - i0 for _, i0, i1 in piece) for piece in pieces]
    col0 = [pair_column(piece[0][1], piece[0][0]) for piece in pieces]
    group_of = [piece[0][0] // GROUP for piece in pieces]
    first_piece = [group_of.index(g) for g in range(NGROUP)]
    chunk_of = [-(-(col0[k] + width[k]) * EMB // CW) - 1 for k in range(NP)]

    def count(kind, t, k):
        n = sum(kinds[s].count(kind) for s in range(t))
        return n + kinds[t][:k + 1].count(kind)

    with ExitStack() as ctx:
        def sb(name, shape, dt=FP32):
            return ctx.enter_context(nc.sbuf_tensor(name, shape, dt))

        def psum(name, shape):
            return ctx.enter_context(nc.psum_tensor(name, shape, FP32))

        def sem(name):
            return ctx.enter_context(nc.semaphore(name))

        ksplit = sb("ksplit", [P, KCOLS], FP32R)
        early = sb("early", [P, max(RAWS * HW, A1 * D1 + A2 * D2)])
        kraw = early[:, 0:RAWS * HW].rearrange("p (s n) -> p s n", s=RAWS)
        w1_sb = early[:, 0:A1 * D1].rearrange("p (a m) -> p a m", a=A1)
        w2_sb = early[:, A1 * D1:A1 * D1 + A2 * D2].rearrange("p (a m) -> p a m", a=A2)
        ids_sb = sb("ids_sb", [P, TILES, FIELDS], INT32)
        emb = sb("emb", [P, 2, FIELDS, EMB])
        twice = sb("twice", [P, 2, GROUP, 2, EMB])
        qhi = sb("qhi", [P, QS, GROUP * P], FP32R)
        qlo = sb("qlo", [P, QS, GROUP * P], FP32R)
        prod = sb("prod", [P, PRODS, PIECE])
        z = sb("z", [P, 2, D1])
        ident = sb("ident", [P, P])
        w3_sb = sb("w3_sb", [P, M2])
        b1_sb = sb("b1_sb", [P, M1])
        b2_sb = sb("b2_sb", [P, M2])
        act_t = sb("act_t", [P, D1])
        h1_t = sb("h1_t", [P, D1])
        y_sb = sb("y_sb", [1, 2, P])

        ps_t = psum("ps_t", [P, SLOTS, PIECE])
        ps_q = psum("ps_q", [P, GROUP * P])
        ps_m = psum("ps_m", [P, BANK])

        ids_in = sem("ids_in")
        ident_sem = sem("ident_sem")
        weights_in = sem("weights_in")
        dense_in = [sem(f"dense_in{b}") for b in range(2)]
        raw_in = [sem(f"raw_in{s}") for s in range(RAWS)]
        emb_in = [[sem(f"emb_in{b}_{g}") for g in range(NGROUP)] for b in range(2)]
        khi_done = sem("khi_done")
        klo_done = sem("klo_done")
        twice_in = [sem(f"twice_in{b}") for b in range(2)]
        turned = sem("turned")
        qhi_done = sem("qhi_done")
        qlo_done = sem("qlo_done")
        pairs_done = sem("pairs_done")
        mult_done = sem("mult_done")
        vsum_done = sem("vsum_done")
        asum_done = sem("asum_done")
        tsum_done = sem("tsum_done")
        gsum_step = sem("gsum_step")
        tfinal_done = sem("tfinal_done")
        gfinal_done = sem("gfinal_done")
        tower_mm = sem("tower_mm")
        tower_act = sem("tower_act")
        y_stored = [sem(f"y_stored{b}") for b in range(2)]

        def side_steps(t, k):
            steps = []
            if t < TILES and k - T_LAG >= 0 and kinds[t][k - T_LAG] == "T":
                steps.append(("T", t, k - T_LAG))
            if t > 0 and k < T_LAG and kinds[t - 1][NP + k - T_LAG] == "T":
                steps.append(("T", t - 1, NP + k - T_LAG))
            if t > 0 and k in TOWER_AT:
                steps.append(("M", t - 1, TOWER_AT.index(k)))
            return steps

        users = [u for t in range(TILES + 1) for k in range(NP if t < TILES else TOWER_AT[-1] + 1)
                 for u in side_steps(t, k)]
        assert len(set(users)) == len(users)

        def wait_ps_m_free(pe, user):
            n = users.index(user)
            if n == 0:
                return
            kind, t, k = users[n - 1]
            if kind == "T":
                pe.wait_ge(tfinal_done, count("T", t, k))
            else:
                pe.wait_ge(tower_act, t * TOWER + k + 1)

        K_AHEAD = 4

        def chunks_at(k):
            if k < 0:
                return range(0, K_AHEAD)
            return range(K_AHEAD + k, K_AHEAD + k + 1) if K_AHEAD + k < KCHUNK else range(0)

        def wait_emb(eng, t, g):
            eng.wait_ge(emb_in[t % 2][g], 16 * GROUP * (t // 2 + 1))

        TURN_AT = [{0: 1, 2: 2, 5: 3, 9: 4, 14: 5, 20: 6, 27: 7} if t == 0 else
                   {1: 3, 5: 4, 9: 5, 14: 6, 20: 7} for t in range(TILES)]
        TURN_AT = [{k: t * NGROUP + g for k, g in at.items()} for t, at in enumerate(TURN_AT)]
        for t, at in enumerate(TURN_AT):
            if t + 1 < TILES:
                at.update({k: (t + 1) * NGROUP + g for k, g in {31: 0, 35: 1, 39: 2}.items()})
        HALVINGS = (EMB // PART).bit_length() - 1

        block = ctx.enter_context(nc.Block())

        @block.sync
        def _(sp):
            def load_chunk(c):
                if c >= RAWS:
                    sp.wait_ge(klo_done, c - RAWS + 1)
                sp.dma_start(kraw[:, c % RAWS, :], k_raw[c]).then_inc(raw_in[c % RAWS], 16)

            def double_rows(n):
                t, g = divmod(n, NGROUP)
                wait_emb(sp, t, g)
                if n >= 2:
                    sp.wait_ge(turned, n - 1)
                src = emb[:, t % 2, GROUP * g:GROUP * (g + 1), :]
                for copy in range(2):
                    sp.dma_start(twice[:, n % 2, :, copy, :], src).then_inc(twice_in[n % 2], 16)

            def load_dense(t):
                if t >= 2:
                    sp.wait_ge(tower_mm, (t - 2) * TOWER + 1)
                sp.dma_start(z[:, t % 2, NPAIR:NPAIR + NDENSE], dense[:, t]).then_inc(dense_in[t % 2], 16)

            def store_y(t):
                sp.wait_ge(tower_act, (t + 1) * TOWER)
                sp.dma_start(y_out[:, t * P:(t + 1) * P], y_sb[:, t % 2, :]).then_inc(y_stored[t % 2], 16)

            sp.dma_start(ids_sb[:], ids).then_inc(ids_in, 16)
            for c in range(RAWS):
                load_chunk(c)
            sp.dma_start(ident[:], ident_in).then_inc(ident_sem, 16)
            sp.dma_start(w3_sb[:], w3).then_inc(weights_in, 16)
            sp.dma_start(b1_sb[:], b1).then_inc(weights_in, 16)
            sp.dma_start(b2_sb[:], b2).then_inc(weights_in, 16)
            load_dense(0)
            load_dense(1)
            double_rows(0)
            load_chunk(RAWS)
            double_rows(1)
            for t in range(TILES):
                for k in range(NP):
                    if t == 0 and RAWS + 1 + k < KCHUNK:
                        load_chunk(RAWS + 1 + k)
                    if t == 0 and RAWS + 1 + k == KCHUNK:
                        sp.wait_ge(klo_done, KCHUNK)
                        sp.dma_start(w1_sb, w1).then_inc(weights_in, 16)
                        sp.dma_start(w2_sb, w2).then_inc(weights_in, 16)
                    n = TURN_AT[t].get(k + 1)
                    if n is not None and n < TILES * NGROUP:
                        double_rows(n)
                    if t > 0 and k == TOWER_AT[-1] + 1:
                        store_y(t - 1)
                    if t >= 1 and t + 1 < TILES and k == TOWER_AT[0] + 1:
                        load_dense(t + 1)
            store_y(TILES - 1)
            sp.wait_ge(y_stored[0], 16 * ((TILES + 1) // 2))
            sp.wait_ge(y_stored[1], 16 * (TILES // 2))

        @block.gpsimd
        def _(pool):
            steps = [0]

            def gather(t, f):
                if t >= 2 and f == 0:
                    pool.wait_ge(mult_done, (t - 1) * NP)
                pool.indirect_dma_start(
                    emb[:, t % 2, f, :], None, tables[f],
                    bass.IndirectOffsetOnAxis(ap=ids_sb[:, t, f:f + 1], axis=0),
                ).then_inc(emb_in[t % 2][f // GROUP], 16)

            def halve(t, k):
                pool.wait_ge(mult_done, t * NP + k + 1)
                v = prod[:, (t * NP + k) % PRODS, 0:width[k] * EMB].rearrange("p (n e) -> p n e", e=EMB)
                w = EMB // 2
                while w >= PART:
                    if w < EMB // 2:
                        pool.wait_ge(gsum_step, steps[0])
                    pool.tensor_tensor(v[:, :, 0:w], v[:, :, 0:w], v[:, :, w:2 * w], ALU.add).then_inc(gsum_step, 1)
                    steps[0] += 1
                    w //= 2

            pool.wait_ge(ids_in, 16)
            for f in range(FIELDS):
                gather(0, f)
            for t in range(TILES):
                for k in range(NP):
                    if kinds[t][k] == "G":
                        halve(t, k)
                    if t + 1 < TILES:
                        for f in range(k * FIELDS // NP, (k + 1) * FIELDS // NP):
                            gather(t + 1, f)

        @block.scalar
        def _(act):
            def split_chunk(c):
                act.wait_ge(raw_in[c % RAWS], 16 * (c // RAWS + 1))
                for half in range(2):
                    o = c * CW + half * HW
                    rows = slice(half * 64, half * 64 + 64)
                    last = act.activation(ksplit[rows, o:o + HW], kraw[rows, c % RAWS, :], ACT.Copy)
                last.then_inc(khi_done, 1)

            def high_q(n):
                t, g = divmod(n, NGROUP)
                act.wait_ge(turned, n + 1)
                if n >= QS:
                    s, h = divmod(n - QS, NGROUP)
                    act.wait_ge(pairs_done, s * NP + (first_piece[h + 1] if h + 1 < NGROUP else NP))
                act.activation(qhi[:, n % QS], ps_q[:], ACT.Copy).then_inc(qhi_done, 1)

            def tower(t, step):
                act.wait_ge(tower_mm, t * TOWER + step + 1)
                if step == 0:
                    last = act.activation(act_t[:], ps_m[:], ACT.Copy)
                elif step == 1:
                    act.wait_ge(weights_in, 80)
                    for m in range(M1):
                        last = act.activation(h1_t[:, m * P:(m + 1) * P], ps_m[:, m * P:(m + 1) * P],
                                              ACT.Relu, bias=b1_sb[:, m:m + 1])
                elif step == 2:
                    for m in range(M2):
                        last = act.activation(act_t[:, m * P:(m + 1) * P], ps_m[:, m * P:(m + 1) * P],
                                              ACT.Relu, bias=b2_sb[:, m:m + 1])
                else:
                    if t >= 2:
                        act.wait_ge(y_stored[t % 2], 16 * (t // 2))
                    last = act.activation(y_sb[:, t % 2, :], ps_m[0:1, 0:P], ACT.Copy)
                last.then_inc(tower_act, 1)

            def sum_piece(t, k):
                act.wait_ge(mult_done, t * NP + k + 1)
                for c in range(width[k]):
                    src = prod[:, (t * NP + k) % PRODS, c * EMB:(c + 1) * EMB]
                    last = act.activation(src, src, ACT.Copy, accum_out=z[:, t % 2, col0[k] + c:col0[k] + c + 1])
                last.then_inc(asum_done, 1)

            for c in chunks_at(-1):
                split_chunk(c)
            high_q(0)
            high_q(1)
            for t in range(TILES):
                for k in range(NP):
                    if k + 1 in TURN_AT[t]:
                        high_q(TURN_AT[t][k + 1])
                    if t > 0 and k + 1 in TOWER_AT:
                        tower(t - 1, TOWER_AT.index(k + 1))
                    if t == 0:
                        for c in chunks_at(k):
                            split_chunk(c)
                    if kinds[t][k] == "A":
                        sum_piece(t, k)
            for step in range(TOWER):
                tower(TILES - 1, step)

        @block.vector
        def _(dve):
            def split_chunk(c):
                dve.wait_ge(khi_done, c + 1)
                for half in range(2):
                    o = c * CW + half * HW
                    rows = slice(half * 64, half * 64 + 64)
                    other = slice(64 - half * 64, 128 - half * 64)
                    last = dve.tensor_tensor(ksplit[other, o:o + HW], kraw[rows, c % RAWS, :],
                                             ksplit[rows, o:o + HW], ALU.subtract)
                last.then_inc(klo_done, 1)

            def low_q(n):
                dve.wait_ge(qhi_done, n + 1)
                dve.tensor_tensor(qlo[:, n % QS], ps_q[:], qhi[:, n % QS], ALU.subtract).then_inc(qlo_done, 1)

            def multiply(t, k):
                n = t * NP + k
                if t >= 2 and k == 0:
                    dve.wait_ge(tower_mm, (t - 2) * TOWER + 1)
                if n >= PRODS:
                    s, h = divmod(n - PRODS, NP)
                    done = {"V": vsum_done, "A": asum_done, "T": tsum_done, "G": gfinal_done}[kinds[s][h]]
                    dve.wait_ge(done, count(kinds[s][h], s, h))
                dve.wait_ge(pairs_done, n + 1)
                o = 0
                for j, i0, i1 in pieces[k]:
                    w = (i1 - i0) * EMB
                    last = dve.tensor_tensor(
                        prod[:, n % PRODS, o:o + w], ps_t[:, n % SLOTS, o:o + w],
                        emb[:, t % 2, i0:i1, :].rearrange("p i e -> p (i e)"), ALU.mult)
                    o += w
                last.then_inc(mult_done, 1)

            def sum_piece(t, k):
                dve.wait_ge(mult_done, t * NP + k + 1)
                src = prod[:, (t * NP + k) % PRODS, 0:width[k] * EMB].rearrange("p (n e) -> p n e", e=EMB)
                dve.tensor_reduce(z[:, t % 2, col0[k]:col0[k] + width[k]], src, AX_X, ALU.add).then_inc(vsum_done, 1)

            def finish_sum(t, k):
                dve.wait_ge(tsum_done, count("T", t, k))
                src = ps_m[:, 0:width[k] * PART].rearrange("p (n r) -> p n r", r=PART)
                dve.tensor_reduce(z[:, t % 2, col0[k]:col0[k] + width[k]], src, AX_X, ALU.add).then_inc(tfinal_done, 1)

            def finish_halved(t, k):
                dve.wait_ge(gsum_step, HALVINGS * count("G", t, k))
                src = prod[:, (t * NP + k) % PRODS, 0:width[k] * EMB].rearrange("p (n e) -> p n e", e=EMB)
                dve.tensor_reduce(z[:, t % 2, col0[k]:col0[k] + width[k]], src[:, :, 0:PART],
                                  AX_X, ALU.add).then_inc(gfinal_done, 1)

            for c in chunks_at(-1):
                split_chunk(c)
            low_q(0)
            for t in range(TILES):
                for k in range(NP):
                    multiply(t, k)
                    if t == 0:
                        for c in chunks_at(k):
                            split_chunk(c)
                    for lag, kind, do in ((1, "V", sum_piece), (F_LAG, "T", finish_sum), (G_LAG, "G", finish_halved)):
                        s, h = divmod(t * NP + k - lag, NP)
                        if s >= 0 and kinds[s][h] == kind:
                            do(s, h)
                    if k in TURN_AT[t]:
                        low_q(TURN_AT[t][k])
            t = TILES - 1
            for lag, kind, do in ((G_LAG, "G", finish_halved), (F_LAG, "T", finish_sum), (1, "V", sum_piece)):
                for h in range(NP - lag, NP):
                    if kinds[t][h] == kind:
                        do(t, h)

        @block.tensor
        def _(pe):
            def turn(n):
                pe.wait_ge(twice_in[n % 2], 32 * (n // 2 + 1))
                if n >= 1:
                    pe.wait_ge(qlo_done, n)
                for f in range(GROUP):
                    last = pe.transpose(ps_q[:, f * P:(f + 1) * P],
                                        twice[:, n % 2, f].rearrange("p a e -> p (a e)"), ident[:])
                last.then_inc(turned, 1)

            def bilinear(t, k):
                n = t * NP + k
                if k == first_piece[group_of[k]]:
                    pe.wait_ge(qlo_done, t * NGROUP + group_of[k] + 1)
                if t == 0:
                    pe.wait_ge(klo_done, chunk_of[k] + 1)
                if n >= SLOTS:
                    pe.wait_ge(mult_done, n - SLOTS + 1)
                q = (t * NGROUP + group_of[k]) % QS
                o = 0
                for j, i0, i1 in pieces[k]:
                    f = j % GROUP
                    i = i0
                    while i < i1:
                        w = min((i1 - i) * EMB, BANK - o % BANK)
                        src = pair_column(i, j) * EMB
                        dst = ps_t[:, n % SLOTS, o:o + w]
                        pe.matmul(dst, qhi[:, q, f * P:(f + 1) * P], ksplit[:, src:src + w],
                                  start=True, stop=False)
                        last = pe.matmul(dst, qlo[:, q, f * P:(f + 1) * P], ksplit[:, src:src + w],
                                         start=False, stop=True)
                        o += w
                        i += w // EMB
                last.then_inc(pairs_done, 1)

            def sum_piece(t, k):
                wait_ps_m_free(pe, ("T", t, k))
                pe.wait_ge(mult_done, t * NP + k + 1)
                w = width[k]
                src = prod[:, (t * NP + k) % PRODS, 0:w * EMB].rearrange("p (n s r) -> p s n r", n=w, r=PART)
                dst = ps_m[:, 0:w * PART].rearrange("p (n r) -> p n r", r=PART)
                for s in range(EMB // PART):
                    last = pe.matmul(dst, ident[:], src[:, s], start=(s == 0), stop=(s == EMB // PART - 1))
                last.then_inc(tsum_done, 1)

            def tower(t, step):
                wait_ps_m_free(pe, ("M", t, step))
                if step == 0:
                    pe.wait_ge(vsum_done, count("V", t, NP - 1))
                    pe.wait_ge(asum_done, count("A", t, NP - 1))
                    pe.wait_ge(tfinal_done, count("T", t, NP - 1))
                    pe.wait_ge(gfinal_done, count("G", t, NP - 1))
                    pe.wait_ge(dense_in[t % 2], 16 * (t // 2 + 1))
                    for a in range(A1):
                        last = pe.transpose(ps_m[:, a * P:(a + 1) * P], z[:, t % 2, a * P:(a + 1) * P], ident[:])
                elif step == 1:
                    pe.wait_ge(weights_in, 80)
                    pe.wait_ge(tower_act, t * TOWER + step)
                    for m in range(M1):
                        for a in range(A1):
                            last = pe.matmul(ps_m[:, m * P:(m + 1) * P], w1_sb[:, a, m * P:(m + 1) * P],
                                             act_t[:, a * P:(a + 1) * P], start=(a == 0), stop=(a == A1 - 1))
                elif step == 2:
                    pe.wait_ge(tower_act, t * TOWER + step)
                    for m in range(M2):
                        for a in range(A2):
                            last = pe.matmul(ps_m[:, m * P:(m + 1) * P], w2_sb[:, a, m * P:(m + 1) * P],
                                             h1_t[:, a * P:(a + 1) * P], start=(a == 0), stop=(a == A2 - 1))
                else:
                    pe.wait_ge(tower_act, t * TOWER + step)
                    for a in range(M2):
                        last = pe.matmul(ps_m[0:1, 0:P], w3_sb[:, a:a + 1], act_t[:, a * P:(a + 1) * P],
                                         start=(a == 0), stop=(a == M2 - 1))
                last.then_inc(tower_mm, 1)

            def side(t, k):
                for kind, s, what in side_steps(t, k):
                    (sum_piece if kind == "T" else tower)(s, what)

            pe.wait_ge(ident_sem, 16)
            turn(0)
            for t in range(TILES):
                for k in range(NP):
                    bilinear(t, k)
                    if k in TURN_AT[t]:
                        turn(TURN_AT[t][k])
                    side(t, k)
            for k in range(TOWER_AT[-1] + 1):
                side(TILES, k)


def kernel(dense_ctx, ids, W_top1, b_top1, W_top2, b_top2, W_top3, L0_rec_kernel, **tbls):
    import numpy as np
    import concourse.bacc as bacc
    from concourse.bass_utils import run_bass_kernel_spmd

    batch = ids.shape[0]
    tiles = batch // P
    row, col = np.triu_indices(FIELDS, k=1)
    order = np.lexsort((row, col))
    k = np.asarray(L0_rec_kernel)[:, order, :].reshape(EMB, KCHUNK, 2, HW)
    w1 = np.asarray(W_top1)
    w1 = np.concatenate([w1[:NPAIR][order], w1[NPAIR:]], axis=0)
    w2 = np.asarray(W_top2)

    def by_partition(a):
        return np.ascontiguousarray(a.reshape(-1, P, a.shape[1]).transpose(1, 0, 2))

    ins = {
        "dense": by_partition(np.asarray(dense_ctx)),
        "ids": by_partition(np.asarray(ids)),
        **{f"tbl_{f}": np.ascontiguousarray(tbls[f"tbl_{f}"]) for f in range(FIELDS)},
        "k_raw": np.ascontiguousarray(k.transpose(1, 2, 0, 3).reshape(KCHUNK, P, HW)),
        "w1": by_partition(w1),
        "b1": np.ascontiguousarray(np.asarray(b_top1).reshape(-1, P).T),
        "w2": by_partition(w2),
        "b2": np.ascontiguousarray(np.asarray(b_top2).reshape(-1, P).T),
        "w3": np.ascontiguousarray(np.asarray(W_top3).reshape(-1, P).T),
        "identity": np.eye(P, dtype=np.float32),
    }
    nc = bacc.Bacc("TRN2", target_bir_lowering=False, num_devices=1)
    ap = {n: nc.dram_tensor(n, a.shape, mybir.dt.from_np(a.dtype), kind="ExternalInput").ap() for n, a in ins.items()}
    y = nc.dram_tensor("y", (1, batch), FP32, kind="ExternalOutput").ap()
    dlrm_tower(nc, ap["dense"], ap["ids"], [ap[f"tbl_{f}"] for f in range(FIELDS)], ap["k_raw"], ap["w1"], ap["b1"],
               ap["w2"], ap["b2"], ap["w3"], ap["identity"], y)
    out = run_bass_kernel_spmd(nc, [ins], core_ids=[0])
    return out.results[0]["y"].reshape(batch, 1)
```

```python
from contextlib import ExitStack

import concourse.bass as bass
from concourse import mybir

FP32 = mybir.dt.float32
FP32R = mybir.dt.float32r
INT32 = mybir.dt.int32
ALU = mybir.AluOpType
ACT = mybir.ActivationFunctionType
AX_X = mybir.AxisListType.X

P = 128
FIELDS = 32
EMB = 64
NPAIR = FIELDS * (FIELDS - 1) // 2
GROUP = 4
NGROUP = FIELDS // GROUP
KCOLS = NPAIR * EMB
KCHUNK = 16
CW = KCOLS // KCHUNK
HW = CW // 2
BANK = 512
PIECE = 2 * BANK
SLOTS = 3
PRODS = 6
RAWS = 4
QS = 4
PART = 8
SCALAR_SHARE = [0.251, 0.36, 0.36, 0.297]
V_WEIGHT = [3.0, 3.0, 2.6, 3.8]
FIRST_GROUP = 8.5
GROUP_PERIOD = 3.6
HI_COST = 1.84
LO_COST = 1.1
MOVE_COST = 3.7
CHUNK_PERIOD = 2.0
PIECE_COST = 1.7
SUM_COST = 1.1
T_WEIGHT = [0.0, 0.4, -0.4, 0.8]
G_WEIGHT = [1.2, 0.4, 1.2, -2.4] 
T_APART = 3


def pair_column(i, j):
    return j * (j - 1) // 2 + i


def plan_pieces():
    edges = [0, 6] + list(range(16, NPAIR + 1, 16))
    columns = [(i, j) for j in range(FIELDS) for i in range(j)]
    pieces = []
    for lo, hi in zip(edges, edges[1:]):
        runs = []
        for i, j in columns[lo:hi]:
            if runs and runs[-1][0] == j:
                runs[-1][2] = i + 1
            else:
                runs.append([j, i, i + 1])
        pieces.append(runs)
    return pieces


def plan_reductions(pieces, tile, tiles, busy):
    last = tile == tiles - 1
    clock, tensor, pool, taken = 0.0, 0.0, 0.0, -9
    kinds, shares = [], []
    for k, piece in enumerate(pieces):
        w = sum(i1 - i0 for _, i0, i1 in piece)
        a = round(w * SCALAR_SHARE[tile])
        n = w - a
        clock += 0.0667 * w + 0.068 * len(piece) + (0.0 if tile else 0.6)
        tensor = max(tensor, clock - 2.0) + 0.055 * w + (0.25 if tile or last else 0.1)
        pool = max(pool, clock - 1.0) + (0.0 if last else 0.79)
        cost_t, cost_g = 0.11 * n + 0.2, 0.125 * n + 0.5
        options = [(0.068 + 0.0667 * n + V_WEIGHT[tile], "V")]
        if n >= 6 and k not in busy and k - taken >= T_APART:
            options.append((max(tensor, clock) + cost_t - clock + T_WEIGHT[tile], "T"))
        if n >= 6 and not (last and k >= len(pieces) - 4):
            options.append((max(pool, clock) + cost_g - clock + G_WEIGHT[tile], "G"))
        kind = "V" if last and k >= len(pieces) - 2 else min(options)[1]
        if kind == "V":
            clock += 0.068 + 0.0667 * n
        elif kind == "T":
            tensor, taken = max(tensor, clock) + cost_t, k
            clock += 0.068 + 0.0083 * n
        else:
            pool = max(pool, clock) + cost_g
            clock += 0.068 + 0.0083 * n
        kinds.append(kind)
        shares.append(a)
    return kinds, shares


def plan_start(pieces):
    order = {e: [] for e in ("tensor", "scalar", "vector")}
    turn = [FIRST_GROUP + GROUP_PERIOD * g for g in range(NGROUP)]
    low, mult, split = [], [], []
    clock = scalar = 0.0
    while len(mult) < len(pieces):
        c, g, k = len(split), len(low), len(mult)
        ready = []
        if g < NGROUP:
            ready.append((turn[g] + 1.4, 0, "group"))
        group = pieces[k][-1][0] // GROUP
        chunk = (pair_column(pieces[k][-1][2] - 1, pieces[k][-1][0]) * EMB) // CW
        if group < g and chunk < c:
            start = max(low[group], split[chunk] + MOVE_COST, mult[k - SLOTS] if k >= SLOTS else 0.0) + 0.1
            ready.append((start + PIECE_COST, 1, "piece"))
        if c < KCHUNK:
            load = 2.5 if c < RAWS else split[c - RAWS] + MOVE_COST
            arrive = max(load + 2.2, 4.6 + CHUNK_PERIOD * c)
            ready.append((max(arrive, scalar) + HI_COST, 2, "chunk"))
        now = [r for r in ready if r[0] <= clock]
        at, _, what = min(now, key=lambda r: r[1]) if now else min(ready)
        clock = max(clock, at)
        if what == "group":
            order["tensor"].append((turn[g], "group", g))
            order["scalar"].append((turn[g] + 0.9, "group", g))
            clock += 0.6
            low.append(clock)
        elif what == "piece":
            order["tensor"].append((start, "piece", k))
            clock += 0.0667 * sum(i1 - i0 for _, i0, i1 in pieces[k]) + 0.07 * len(pieces[k])
            order["scalar"].append((clock, "piece", k))
            mult.append(clock)
            clock += SUM_COST
        else:
            scalar = max(arrive, scalar) + HI_COST
            order["scalar"].append((scalar - HI_COST, "chunk", c))
            clock += LO_COST
            split.append(clock)
        order["vector"].append((at, what, {"group": g, "piece": k, "chunk": c}[what]))
    assert len(split) == KCHUNK and len(low) == NGROUP
    return {e: [(what, n) for _, what, n in sorted(o, key=lambda x: x[0])] for e, o in order.items()}


def dlrm_tower(nc, dense, ids, tables, k_raw, w1, b1, w2, b2, w3, ident_in, y_out):
    TILES = ids.shape[1]
    D1 = w1.shape[2]
    D2 = w2.shape[2]
    A1, A2 = w1.shape[1], w2.shape[1]
    M1, M2 = D1 // P, D2 // P
    NDENSE = dense.shape[2]

    TOWER = 4
    TOWER_AT = [4, 9, 14, 19]
    T_LAG = 3
    Q_LAG = 1
    G_LAG = 4
    F_LAG = 3
    NOT_T = [at - T_LAG - d for at in TOWER_AT for d in range(T_APART)]

    pieces = plan_pieces()
    NP = len(pieces)
    plans = [plan_reductions(pieces, t, TILES, NOT_T if t else []) for t in range(TILES)]
    kinds = [plan[0] for plan in plans]
    shares = [plan[1] for plan in plans]
    width = [sum(i1 - i0 for _, i0, i1 in piece) for piece in pieces]
    col0 = [pair_column(piece[0][1], piece[0][0]) for piece in pieces]
    last_piece = [max(k for k in range(NP) if pieces[k][0][0] // GROUP <= g) for g in range(NGROUP)]
    chunk_of = [-(-(col0[k] + width[k]) * EMB // CW) - 1 for k in range(NP)]

    def count(kind, t, k):
        n = sum(kinds[s].count(kind) for s in range(t))
        return n + kinds[t][:k + 1].count(kind)

    assert all(a > 0 for share in shares for a in share)
    rest = [[w - a for w, a in zip(width, share)] for share in shares]

    with ExitStack() as ctx:
        def sb(name, shape, dt=FP32):
            return ctx.enter_context(nc.sbuf_tensor(name, shape, dt))

        def psum(name, shape):
            return ctx.enter_context(nc.psum_tensor(name, shape, FP32))

        def sem(name):
            return ctx.enter_context(nc.semaphore(name))

        ksplit = sb("ksplit", [P, KCOLS], FP32R)
        early = sb("early", [P, max(RAWS * HW, A1 * D1 + A2 * D2)])
        kraw = early[:, 0:RAWS * HW].rearrange("p (s n) -> p s n", s=RAWS)
        w1_sb = early[:, 0:A1 * D1].rearrange("p (a m) -> p a m", a=A1)
        w2_sb = early[:, A1 * D1:A1 * D1 + A2 * D2].rearrange("p (a m) -> p a m", a=A2)
        ids_sb = sb("ids_sb", [P, TILES, FIELDS], INT32)
        emb = sb("emb", [P, 2, FIELDS, EMB])
        qhi = sb("qhi", [P, QS, GROUP * P], FP32R)
        qlo = sb("qlo", [P, QS, GROUP * P], FP32R)
        prod = sb("prod", [P, PRODS, PIECE])
        z = sb("z", [P, 2, D1])
        ident = sb("ident", [P, P])
        w3_sb = sb("w3_sb", [P, M2])
        b1_sb = sb("b1_sb", [P, M1])
        b2_sb = sb("b2_sb", [P, M2])
        act_t = sb("act_t", [P, D1])
        h1_t = sb("h1_t", [P, D1])
        y_sb = sb("y_sb", [1, 2, P])

        ps_t = psum("ps_t", [P, SLOTS, PIECE])
        ps_q = psum("ps_q", [P, GROUP * P])
        ps_m = psum("ps_m", [P, BANK])

        ids_in = sem("ids_in")
        ident_sem = sem("ident_sem")
        weights_in = sem("weights_in")
        dense_in = [sem(f"dense_in{b}") for b in range(2)]
        raw_in = [sem(f"raw_in{s}") for s in range(RAWS)]
        emb_in = [[sem(f"emb_in{b}_{g}") for g in range(NGROUP)] for b in range(2)]
        khi_placed = sem("khi_placed")
        klo_done = sem("klo_done")
        lo_moved = [sem(f"lo_moved{s}") for s in range(RAWS)]
        turned = sem("turned")
        qhi_done = sem("qhi_done")
        qlo_done = sem("qlo_done")
        pairs_done = sem("pairs_done")
        mult_done = sem("mult_done")
        vsum_done = sem("vsum_done")
        asum_done = sem("asum_done")
        tsum_done = sem("tsum_done")
        gsum_step = sem("gsum_step")
        tfinal_done = sem("tfinal_done")
        gfinal_done = sem("gfinal_done")
        tower_mm = sem("tower_mm")
        tower_act = sem("tower_act")
        y_stored = [sem(f"y_stored{b}") for b in range(2)]

        def side_steps(t, k):
            steps = []
            if t < TILES and k - T_LAG >= 0 and kinds[t][k - T_LAG] == "T":
                steps.append(("T", t, k - T_LAG))
            if t > 0 and k < T_LAG and kinds[t - 1][NP + k - T_LAG] == "T":
                steps.append(("T", t - 1, NP + k - T_LAG))
            if t > 0 and k in TOWER_AT:
                steps.append(("M", t - 1, TOWER_AT.index(k)))
            return steps

        users = [u for t in range(TILES + 1) for k in range(NP if t < TILES else TOWER_AT[-1] + 1)
                 for u in side_steps(t, k)]
        assert len(set(users)) == len(users)

        def wait_ps_m_free(pe, user):
            n = users.index(user)
            if n == 0:
                return
            kind, t, k = users[n - 1]
            if kind == "T":
                pe.wait_ge(tfinal_done, count("T", t, k))
            else:
                pe.wait_ge(tower_act, t * TOWER + k + 1)

        start = plan_start(pieces)

        def wait_emb(eng, t, g):
            eng.wait_ge(emb_in[t % 2][g], 16 * GROUP * (t // 2 + 1))

        TURN_AT, LOW_AT = [{} for _ in range(TILES)], [{} for _ in range(TILES)]
        for t in range(TILES):
            if t > 0:
                for g, k in {3: 0, 4: 4, 5: 8, 6: 12, 7: 17}.items():
                    TURN_AT[t][k] = LOW_AT[t][k + Q_LAG] = t * NGROUP + g
            if t + 1 < TILES:
                for g, k in {0: 22, 1: 25, 2: 28}.items():
                    TURN_AT[t][k] = LOW_AT[t][k + Q_LAG] = (t + 1) * NGROUP + g
        HALVINGS = (EMB // PART).bit_length() - 1

        block = ctx.enter_context(nc.Block())

        @block.sync
        def _(sp):
            def load_chunk(c):
                if c >= RAWS:
                    sp.wait_ge(lo_moved[c % RAWS], 32 * (c // RAWS))
                sp.dma_start(kraw[:, c % RAWS, :], k_raw[c]).then_inc(raw_in[c % RAWS], 16)

            def move_chunk(c):
                sp.wait_ge(klo_done, c + 1)
                for half in range(2):
                    o = c * CW + half * HW
                    rows = slice(half * 64, half * 64 + 64)
                    other = slice(64 - half * 64, 128 - half * 64)
                    sp.dma_start(ksplit[other, o:o + HW].bitcast(FP32),
                                 kraw[rows, c % RAWS, :]).then_inc(lo_moved[c % RAWS], 16)

            sp.dma_start(ids_sb[:], ids).then_inc(ids_in, 16)
            sp.dma_start(ident[:], ident_in).then_inc(ident_sem, 16)
            for c in range(RAWS):
                load_chunk(c)
            for c in range(KCHUNK):
                move_chunk(c)
                if c >= 1 and c - 1 + RAWS < KCHUNK:
                    load_chunk(c - 1 + RAWS)
            for c in range(KCHUNK - RAWS, KCHUNK):
                sp.wait_ge(lo_moved[c % RAWS], 32 * (c // RAWS + 1))
            sp.dma_start(w1_sb, w1).then_inc(weights_in, 16)
            sp.dma_start(w2_sb, w2).then_inc(weights_in, 16)
        @block.gpsimd
        def _(pool):
            steps = [0]

            def gather(t, f):
                if t >= 2 and f == 0:
                    pool.wait_ge(mult_done, (t - 1) * NP)
                pool.indirect_dma_start(
                    emb[:, t % 2, f, :], None, tables[f],
                    bass.IndirectOffsetOnAxis(ap=ids_sb[:, t, f:f + 1], axis=0),
                ).then_inc(emb_in[t % 2][f // GROUP], 16)

            def halve(t, k):
                pool.wait_ge(mult_done, t * NP + k + 1)
                v = prod[:, (t * NP + k) % PRODS, 0:rest[t][k] * EMB].rearrange("p (n e) -> p n e", e=EMB)
                w = EMB // 2
                while w >= PART:
                    if w < EMB // 2:
                        pool.wait_ge(gsum_step, steps[0])
                    pool.tensor_tensor(v[:, :, 0:w], v[:, :, 0:w], v[:, :, w:2 * w], ALU.add).then_inc(gsum_step, 1)
                    steps[0] += 1
                    w //= 2

            pool.wait_ge(ids_in, 16)
            for f in range(FIELDS):
                gather(0, f)
            for t in range(TILES):
                for k in range(NP):
                    if kinds[t][k] == "G":
                        halve(t, k)
                    if t + 1 < TILES:
                        for f in range(k * FIELDS // NP, (k + 1) * FIELDS // NP):
                            gather(t + 1, f)

        @block.scalar
        def _(act):
            def split_chunk(c):
                act.wait_ge(raw_in[c % RAWS], 16 * (c // RAWS + 1))
                o = c * CW
                act.activation(ksplit[:, o:o + HW], kraw[:, c % RAWS, :], ACT.Copy)
                act.activation(ksplit[64:128, o + HW:o + 2 * HW], kraw[64:128, c % RAWS, :],
                               ACT.Copy).then_inc(khi_placed, 1)

            def high_q(n):
                t, g = divmod(n, NGROUP)
                act.wait_ge(turned, n + 1)
                if n >= QS:
                    s, h = divmod(n - QS, NGROUP)
                    act.wait_ge(pairs_done, s * NP + last_piece[h] + 1)
                act.activation(qhi[:, n % QS], ps_q[:], ACT.Copy).then_inc(qhi_done, 1)

            def load_dense(t):
                if t >= 2:
                    act.wait_ge(tower_mm, (t - 2) * TOWER + 1)
                act.dma_start(z[:, t % 2, NPAIR:NPAIR + NDENSE], dense[:, t]).then_inc(dense_in[t % 2], 16)

            def tower(t, step):
                act.wait_ge(tower_mm, t * TOWER + step + 1)
                if step == 0:
                    last = act.activation(act_t[:], ps_m[:], ACT.Copy)
                elif step == 1:
                    act.wait_ge(weights_in, 80)
                    for m in range(M1):
                        last = act.activation(h1_t[:, m * P:(m + 1) * P], ps_m[:, m * P:(m + 1) * P],
                                              ACT.Relu, bias=b1_sb[:, m:m + 1])
                elif step == 2:
                    for m in range(M2):
                        last = act.activation(act_t[:, m * P:(m + 1) * P], ps_m[:, m * P:(m + 1) * P],
                                              ACT.Relu, bias=b2_sb[:, m:m + 1])
                else:
                    if t >= 2:
                        act.wait_ge(y_stored[t % 2], 16 * (t // 2))
                    last = act.activation(y_sb[:, t % 2, :], ps_m[0:1, 0:P], ACT.Copy)
                last.then_inc(tower_act, 1)
                if step == 0 and t + 2 < TILES:
                    load_dense(t + 2)
                if step == TOWER - 1:
                    act.wait_ge(tower_act, (t + 1) * TOWER)
                    act.dma_start(y_out[:, t * P:(t + 1) * P], y_sb[:, t % 2, :]).then_inc(y_stored[t % 2], 16)

            def sum_share(t, k):
                act.wait_ge(mult_done, t * NP + k + 1)
                for c in range(rest[t][k], width[k]):
                    src = prod[:, (t * NP + k) % PRODS, c * EMB:(c + 1) * EMB]
                    last = act.activation(src, src, ACT.Copy, accum_out=z[:, t % 2, col0[k] + c:col0[k] + c + 1])
                last.then_inc(asum_done, 1)

            def piece(t, k):
                if t > 0 and k + 1 in TOWER_AT:
                    tower(t - 1, TOWER_AT.index(k + 1))
                if k in TURN_AT[t]:
                    high_q(TURN_AT[t][k])
                sum_share(t, k)

            for what, n in start["scalar"]:
                if what == "chunk":
                    split_chunk(n)
                elif what == "group":
                    high_q(n)
                else:
                    piece(0, n)
            act.dma_start(w3_sb[:], w3).then_inc(weights_in, 16)
            act.dma_start(b1_sb[:], b1).then_inc(weights_in, 16)
            act.dma_start(b2_sb[:], b2).then_inc(weights_in, 16)
            load_dense(0)
            load_dense(1)
            for t in range(1, TILES):
                for k in range(NP):
                    piece(t, k)
            for step in range(TOWER):
                tower(TILES - 1, step)
            act.wait_ge(y_stored[0], 16 * ((TILES + 1) // 2))
            act.wait_ge(y_stored[1], 16 * (TILES // 2))

        @block.vector
        def _(dve):
            def split_chunk(c):
                dve.wait_ge(khi_placed, c + 1)
                dve.tensor_tensor(kraw[:, c % RAWS, :], kraw[:, c % RAWS, :], ksplit[:, c * CW:c * CW + HW],
                                  ALU.subtract).then_inc(klo_done, 1)

            def low_q(n):
                dve.wait_ge(qhi_done, n + 1)
                dve.tensor_tensor(qlo[:, n % QS], ps_q[:], qhi[:, n % QS], ALU.subtract).then_inc(qlo_done, 1)

            def multiply(t, k):
                n = t * NP + k
                if t >= 2 and k == 0:
                    dve.wait_ge(tower_mm, (t - 2) * TOWER + 1)
                if n >= PRODS:
                    s, h = divmod(n - PRODS, NP)
                    done = {"V": vsum_done, "T": tsum_done, "G": gfinal_done}[kinds[s][h]]
                    dve.wait_ge(done, count(kinds[s][h], s, h))
                    dve.wait_ge(asum_done, n - PRODS + 1)
                dve.wait_ge(pairs_done, n + 1)
                o = 0
                for j, i0, i1 in pieces[k]:
                    w = (i1 - i0) * EMB
                    last = dve.tensor_tensor(
                        prod[:, n % PRODS, o:o + w], ps_t[:, n % SLOTS, o:o + w],
                        emb[:, t % 2, i0:i1, :].rearrange("p i e -> p (i e)"), ALU.mult)
                    o += w
                last.then_inc(mult_done, 1)

            def sum_piece(t, k):
                dve.wait_ge(mult_done, t * NP + k + 1)
                src = prod[:, (t * NP + k) % PRODS, 0:rest[t][k] * EMB].rearrange("p (n e) -> p n e", e=EMB)
                dve.tensor_reduce(z[:, t % 2, col0[k]:col0[k] + rest[t][k]], src, AX_X, ALU.add).then_inc(vsum_done, 1)

            def finish_sum(t, k):
                dve.wait_ge(tsum_done, count("T", t, k))
                src = ps_m[:, 0:rest[t][k] * PART].rearrange("p (n r) -> p n r", r=PART)
                dve.tensor_reduce(z[:, t % 2, col0[k]:col0[k] + rest[t][k]], src, AX_X, ALU.add).then_inc(tfinal_done, 1)

            def finish_halved(t, k):
                dve.wait_ge(gsum_step, HALVINGS * count("G", t, k))
                src = prod[:, (t * NP + k) % PRODS, 0:rest[t][k] * EMB].rearrange("p (n e) -> p n e", e=EMB)
                dve.tensor_reduce(z[:, t % 2, col0[k]:col0[k] + rest[t][k]], src[:, :, 0:PART],
                                  AX_X, ALU.add).then_inc(gfinal_done, 1)

            def piece(t, k):
                multiply(t, k)
                if k in LOW_AT[t]:
                    low_q(LOW_AT[t][k])
                for lag, kind, do in ((1, "V", sum_piece), (F_LAG, "T", finish_sum), (G_LAG, "G", finish_halved)):
                    s, h = divmod(t * NP + k - lag, NP)
                    if s >= 0 and kinds[s][h] == kind:
                        do(s, h)

            for what, n in start["vector"]:
                if what == "chunk":
                    split_chunk(n)
                elif what == "group":
                    low_q(n)
                else:
                    piece(0, n)
            for t in range(1, TILES):
                for k in range(NP):
                    piece(t, k)
            t = TILES - 1
            for lag, kind, do in ((G_LAG, "G", finish_halved), (F_LAG, "T", finish_sum), (1, "V", sum_piece)):
                for h in range(NP - lag, NP):
                    if kinds[t][h] == kind:
                        do(t, h)

        @block.tensor
        def _(pe):
            def turn(n):
                t, g = divmod(n, NGROUP)
                wait_emb(pe, t, g)
                if n >= 1:
                    pe.wait_ge(qlo_done, n)
                for f in range(GROUP):
                    rows = emb[:, t % 2, GROUP * g + f, :]
                    pe.transpose(ps_q[0:EMB, f * P:(f + 1) * P], rows, ident[:])
                    last = pe.matmul(ps_q[EMB:P, f * P:(f + 1) * P], rows, ident[:], start=True, stop=True)
                last.then_inc(turned, 1)

            def bilinear(t, k):
                n = t * NP + k
                pe.wait_ge(qlo_done, t * NGROUP + pieces[k][-1][0] // GROUP + 1)
                if t == 0:
                    for c in range(chunk_of[k - 1] + 1 if k else 0, chunk_of[k] + 1):
                        pe.wait_ge(lo_moved[c % RAWS], 32 * (c // RAWS + 1))
                if n >= SLOTS:
                    pe.wait_ge(mult_done, n - SLOTS + 1)
                o = 0
                for j, i0, i1 in pieces[k]:
                    q = (t * NGROUP + j // GROUP) % QS
                    f = j % GROUP
                    i = i0
                    while i < i1:
                        w = min((i1 - i) * EMB, BANK - o % BANK)
                        src = pair_column(i, j) * EMB
                        dst = ps_t[:, n % SLOTS, o:o + w]
                        pe.matmul(dst, qhi[:, q, f * P:(f + 1) * P], ksplit[:, src:src + w],
                                  start=True, stop=False)
                        last = pe.matmul(dst, qlo[:, q, f * P:(f + 1) * P], ksplit[:, src:src + w],
                                         start=False, stop=True)
                        o += w
                        i += w // EMB
                last.then_inc(pairs_done, 1)

            def sum_piece(t, k):
                wait_ps_m_free(pe, ("T", t, k))
                pe.wait_ge(mult_done, t * NP + k + 1)
                w = rest[t][k]
                src = prod[:, (t * NP + k) % PRODS, 0:w * EMB].rearrange("p (n s r) -> p s n r", n=w, r=PART)
                dst = ps_m[:, 0:w * PART].rearrange("p (n r) -> p n r", r=PART)
                for s in range(EMB // PART):
                    last = pe.matmul(dst, ident[:], src[:, s], start=(s == 0), stop=(s == EMB // PART - 1))
                last.then_inc(tsum_done, 1)

            def tower(t, step):
                wait_ps_m_free(pe, ("M", t, step))
                if step == 0:
                    pe.wait_ge(vsum_done, count("V", t, NP - 1))
                    pe.wait_ge(asum_done, (t + 1) * NP)
                    pe.wait_ge(tfinal_done, count("T", t, NP - 1))
                    pe.wait_ge(gfinal_done, count("G", t, NP - 1))
                    pe.wait_ge(dense_in[t % 2], 16 * (t // 2 + 1))
                    for a in range(A1):
                        last = pe.transpose(ps_m[:, a * P:(a + 1) * P], z[:, t % 2, a * P:(a + 1) * P], ident[:])
                elif step == 1:
                    pe.wait_ge(weights_in, 80)
                    pe.wait_ge(tower_act, t * TOWER + step)
                    for m in range(M1):
                        for a in range(A1):
                            last = pe.matmul(ps_m[:, m * P:(m + 1) * P], w1_sb[:, a, m * P:(m + 1) * P],
                                             act_t[:, a * P:(a + 1) * P], start=(a == 0), stop=(a == A1 - 1))
                elif step == 2:
                    pe.wait_ge(tower_act, t * TOWER + step)
                    for m in range(M2):
                        for a in range(A2):
                            last = pe.matmul(ps_m[:, m * P:(m + 1) * P], w2_sb[:, a, m * P:(m + 1) * P],
                                             h1_t[:, a * P:(a + 1) * P], start=(a == 0), stop=(a == A2 - 1))
                else:
                    pe.wait_ge(tower_act, t * TOWER + step)
                    for a in range(M2):
                        last = pe.matmul(ps_m[0:1, 0:P], w3_sb[:, a:a + 1], act_t[:, a * P:(a + 1) * P],
                                         start=(a == 0), stop=(a == M2 - 1))
                last.then_inc(tower_mm, 1)

            def side(t, k):
                for kind, s, what in side_steps(t, k):
                    (sum_piece if kind == "T" else tower)(s, what)

            def piece(t, k):
                bilinear(t, k)
                if k in TURN_AT[t]:
                    turn(TURN_AT[t][k])
                side(t, k)

            pe.wait_ge(ident_sem, 16)
            for what, n in start["tensor"]:
                if what == "group":
                    turn(n)
                else:
                    piece(0, n)
            for t in range(1, TILES):
                for k in range(NP):
                    piece(t, k)
            for k in range(TOWER_AT[-1] + 1):
                side(TILES, k)


def kernel(dense_ctx, ids, W_top1, b_top1, W_top2, b_top2, W_top3, L0_rec_kernel, **tbls):
    import numpy as np
    import concourse.bacc as bacc
    from concourse.bass_utils import run_bass_kernel_spmd

    batch = ids.shape[0]
    tiles = batch // P
    row, col = np.triu_indices(FIELDS, k=1)
    order = np.lexsort((row, col))
    k = np.asarray(L0_rec_kernel)[:, order, :].reshape(EMB, KCHUNK, 2, HW)
    w1 = np.asarray(W_top1)
    w1 = np.concatenate([w1[:NPAIR][order], w1[NPAIR:]], axis=0)
    w2 = np.asarray(W_top2)

    def by_partition(a):
        return np.ascontiguousarray(a.reshape(-1, P, a.shape[1]).transpose(1, 0, 2))

    ins = {
        "dense": by_partition(np.asarray(dense_ctx)),
        "ids": by_partition(np.asarray(ids)),
        **{f"tbl_{f}": np.ascontiguousarray(tbls[f"tbl_{f}"]) for f in range(FIELDS)},
        "k_raw": np.ascontiguousarray(k.transpose(1, 2, 0, 3).reshape(KCHUNK, P, HW)),
        "w1": by_partition(w1),
        "b1": np.ascontiguousarray(np.asarray(b_top1).reshape(-1, P).T),
        "w2": by_partition(w2),
        "b2": np.ascontiguousarray(np.asarray(b_top2).reshape(-1, P).T),
        "w3": np.ascontiguousarray(np.asarray(W_top3).reshape(-1, P).T),
        "identity": np.eye(P, dtype=np.float32),
    }
    nc = bacc.Bacc("TRN2", target_bir_lowering=False, num_devices=1)
    ap = {n: nc.dram_tensor(n, a.shape, mybir.dt.from_np(a.dtype), kind="ExternalInput").ap() for n, a in ins.items()}
    y = nc.dram_tensor("y", (1, batch), FP32, kind="ExternalOutput").ap()
    dlrm_tower(nc, ap["dense"], ap["ids"], [ap[f"tbl_{f}"] for f in range(FIELDS)], ap["k_raw"], ap["w1"], ap["b1"],
               ap["w2"], ap["b2"], ap["w3"], ap["identity"], y)
    out = run_bass_kernel_spmd(nc, [ins], core_ids=[0])
    return out.results[0]["y"].reshape(batch, 1)
```
